# Optimizing a Trainium2 kernel written in Bass

```python
import numpy as np
import jax
import jax.numpy as jnp

def _softmax(x, axis=-1):
    return jax.nn.softmax(x, axis=axis)
def _gelu(x):
    return jax.nn.gelu(x, approximate=True)
def _silu(x):
    return jax.nn.silu(x)
def _sigmoid(x):
    return jax.nn.sigmoid(x)
def _layernorm(x, axis=-1, eps=1e-5):
    m = jnp.mean(x, axis=axis, keepdims=True)
    v = jnp.var(x, axis=axis, keepdims=True)
    return (x - m) / jnp.sqrt(v + eps)
def _scatter_add(tgt, idx, src, axis=0):
    return tgt.at[idx].add(src)
def _segment_sum(src, seg, n):
    return jax.ops.segment_sum(src, seg, n)

kernel_name = 'mk_conv_seq_d1_conv_nchw512_a634ad'

def setup_inputs(seed: int = 0):
    np.random.seed(seed)
    _w = jnp.asarray
    def _rec_inputs():
        import jax
        import jax.numpy as jnp
        _gk = jax.random.key(seed)
        x = -7.109e-05 + 0.9999 * jax.random.normal(jax.random.fold_in(_gk, 1), (8, 512, 128, 128), jnp.float32)
        return x
    x = _rec_inputs()
    def _L0_conv_setup():
        import jax, jax.numpy as jnp
        import numpy as np
        CB = 4
        CD = 128
        key = jax.random.key(seed)
        kx, kw = jax.random.split(key)
        x = jax.random.normal(kx, (8, 512, 128, 128), dtype=jnp.float32)
        wc = jax.random.normal(kw, (CB, CD, CD), dtype=jnp.float32) * 0.02
        return {'x': x, 'wc': wc}
    _L0_conv_all = _L0_conv_setup()
    _L0_conv_in = {k: v for k, v in _L0_conv_all.items() if k in ('wc', )}
    del _L0_conv_all

    return {
        "x": x,
        "L0_conv_wc": _L0_conv_in["wc"],
    }

def reference(x, L0_conv_wc):
    import jax
    import jax.numpy as jnp
    def _L0_conv_ref(x, wc):
        import jax, jax.numpy as jnp
        import numpy as np
        CB = 4
        CD = 128
        B, C, H, W = x.shape
        xr = jnp.transpose(x, (0, 2, 3, 1)).reshape(B, H, W, CB, CD)
        out = jnp.einsum('bhwij,ijk->bhwik', xr, wc)
        out = out.reshape(B, H, W, C).transpose(0, 3, 1, 2)
        return jax.nn.gelu(x + out, approximate=False)

    def _gn(v, G=32, eps=1e-5):
        B_, C_, H_, W_ = v.shape
        g = v.reshape(B_, G, C_ // G, H_, W_)
        m = jnp.mean(g, axis=(2, 3, 4), keepdims=True)
        s = jnp.var(g, axis=(2, 3, 4), keepdims=True)
        return ((g - m) / jnp.sqrt(s + eps)).reshape(v.shape)

    def _ln_c(v, eps=1e-6):
        m = jnp.mean(v, axis=1, keepdims=True)
        s = jnp.var(v, axis=1, keepdims=True)
        return (v - m) / jnp.sqrt(s + eps)

    def _ln_t(v, eps=1e-5):
        m = jnp.mean(v, axis=-1, keepdims=True)
        s = jnp.var(v, axis=-1, keepdims=True)
        return (v - m) / jnp.sqrt(s + eps)

    def _to_tokens(v):
        B_, C_, H_, W_ = v.shape
        return v.reshape(B_, C_, H_ * W_).transpose(0, 2, 1)
    def _from_tokens(t, like):
        B_, C_, H_, W_ = like.shape
        return t.transpose(0, 2, 1).reshape(B_, C_, H_, W_)

    x = _L0_conv_ref(x, L0_conv_wc)
    return x


_drawn_inputs = setup_inputs


def setup_inputs(seed=0):
    import zlib

    import numpy as np

    out = dict(_drawn_inputs(seed))
    spreads = {}
    factors = {}
    for name, (base, spread) in spreads.items():
        noise = np.random.default_rng([zlib.crc32(name.encode()), seed]).standard_normal(out[name].shape)
        drawn = base * np.exp(spread * noise) if base else spread * noise
        out[name] = jnp.asarray(drawn.astype(out[name].dtype))
    for name, factor in factors.items():
        out[name] = (out[name] * factor).astype(out[name].dtype)
    return out
```

```python
from contextlib import ExitStack

import concourse.bass as bass
from concourse import mybir


def channel_mix_gelu(nc, x, wc, out):
    fp32 = mybir.dt.float32
    GELU = mybir.ActivationFunctionType.Gelu
    ADD = mybir.AluOpType.add

    BATCH, CHANNELS, HEIGHT, WIDTH = x.shape
    GROUPS, C, _ = wc.shape
    PIXELS = HEIGHT * WIDTH

    TILE = 4096
    BANK = 512
    CHUNK = 2 * BANK
    PSUM_SLOTS = 4
    CHUNKS = TILE // CHUNK
    PER_ROUND = 2
    SLOTS = GROUPS * PER_ROUND
    ROUNDS_PER_IMAGE = PIXELS // (TILE * PER_ROUND)
    ROUNDS = BATCH * ROUNDS_PER_IMAGE
    LAST = ROUNDS - 1
    DMA = 16

    x_tiles = x.rearrange("b (g c) (t h) w -> b t g c (h w)", g=GROUPS, t=PIXELS // TILE)
    out_tiles = out.rearrange("b (g c) (t h) w -> b t g c (h w)", g=GROUPS, t=PIXELS // TILE)

    def dram_tile(tiles, rnd, slot):
        group, turn = slot // PER_ROUND, slot % PER_ROUND
        return tiles[rnd // ROUNDS_PER_IMAGE, (rnd % ROUNDS_PER_IMAGE) * PER_ROUND + turn, group]

    def chunk_number(rnd, slot, chunk):
        return rnd * (SLOTS * CHUNKS) + (slot * CHUNKS + chunk)

    with ExitStack() as ctx:
        weights = ctx.enter_context(nc.sbuf_tensor("weights", [C, GROUPS, C], fp32))
        ring = ctx.enter_context(nc.sbuf_tensor("ring", [C, SLOTS, TILE], fp32))
        products = ctx.enter_context(nc.psum_tensor("products", [C, PSUM_SLOTS, CHUNK], fp32))

        def sem(name):
            return ctx.enter_context(nc.semaphore(name))

        weights_loaded = sem("weights_loaded")
        tile_loaded = [sem(f"tile_loaded_{s}") for s in range(SLOTS)]
        tile_stored = [sem(f"tile_stored_{s}") for s in range(SLOTS)]
        end_loaded = [sem(f"end_loaded_{c}") for c in range(CHUNKS)]
        end_stored = sem("end_stored")
        product_ready = sem("product_ready")
        sum_ready = sem("sum_ready")
        gelu_ready = sem("gelu_ready")

        def columns(chunk):
            return slice(chunk * CHUNK, (chunk + 1) * CHUNK)

        def is_end(rnd, slot):
            return isinstance(rnd, int) and rnd == LAST and slot == SLOTS - 1

        block = ctx.enter_context(nc.Block())

        @block.sync
        def _(sp):
            for s in range(SLOTS):
                sp.dma_start(ring[:, s, :], dram_tile(x_tiles, 0, s)).then_inc(tile_loaded[s], DMA)
            with sp.Fori(1, LAST) as rnd:
                for s in range(SLOTS):
                    sp.wait_ge(tile_stored[s], rnd * DMA)
                    sp.dma_start(ring[:, s, :], dram_tile(x_tiles, rnd, s)).then_inc(tile_loaded[s], DMA)
            for s in range(SLOTS):
                sp.wait_ge(tile_stored[s], LAST * DMA)
                if s < SLOTS - 1:
                    sp.dma_start(ring[:, s, :], dram_tile(x_tiles, LAST, s)).then_inc(tile_loaded[s], DMA)
                else:
                    for c in range(CHUNKS):
                        sp.dma_start(ring[:, s, columns(c)],
                                     dram_tile(x_tiles, LAST, s)[:, columns(c)]).then_inc(end_loaded[c], DMA)
            for s in range(SLOTS - 1):
                sp.wait_ge(tile_stored[s], ROUNDS * DMA)
            sp.wait_ge(end_stored, CHUNKS * DMA)

        @block.tensor
        def _(pe):
            def multiply(rnd, s):
                if not is_end(rnd, s):
                    pe.wait_ge(tile_loaded[s], (rnd + 1) * DMA)
                for c in range(CHUNKS):
                    if is_end(rnd, s):
                        pe.wait_ge(end_loaded[c], DMA)
                    n = chunk_number(rnd, s, c)
                    if not isinstance(rnd, int) or n >= PSUM_SLOTS:
                        pe.wait_ge(sum_ready, n - (PSUM_SLOTS - 1))
                    for bank in range(CHUNK // BANK):
                        first = c * CHUNK + bank * BANK
                        last = nc.tensor.matmul(products[:, c % PSUM_SLOTS, bank * BANK:(bank + 1) * BANK],
                                                weights[:, s // PER_ROUND, :], ring[:, s, first:first + BANK],
                                                start=True, stop=True)
                    last.then_inc(product_ready, 1)

            pe.wait_ge(weights_loaded, DMA)
            for s in range(SLOTS):
                multiply(0, s)
            with pe.Fori(1, LAST) as rnd:
                for s in range(SLOTS):
                    multiply(rnd, s)
            for s in range(SLOTS):
                multiply(LAST, s)

        @block.vector
        def _(dve):
            with dve.Fori(0, ROUNDS) as rnd:
                for s in range(SLOTS):
                    for c in range(CHUNKS):
                        dve.wait_ge(product_ready, chunk_number(rnd, s, c) + 1)
                        nc.vector.tensor_tensor(ring[:, s, columns(c)], products[:, c % PSUM_SLOTS, :],
                                                ring[:, s, columns(c)], ADD).then_inc(sum_ready, 1)

        @block.scalar
        def _(act):
            def activate(rnd, s):
                for c in range(CHUNKS):
                    n = chunk_number(rnd, s, c)
                    act.wait_ge(sum_ready, n + 1)
                    nc.scalar.activation(ring[:, s, columns(c)], ring[:, s, columns(c)],
                                         GELU).then_inc(gelu_ready, 1)
                    if is_end(rnd, s):
                        act.wait_ge(gelu_ready, n + 1)
                        act.dma_start(dram_tile(out_tiles, rnd, s)[:, columns(c)],
                                      ring[:, s, columns(c)]).then_inc(end_stored, DMA)
                if not is_end(rnd, s):
                    act.wait_ge(gelu_ready, n + 1)
                    act.dma_start(dram_tile(out_tiles, rnd, s), ring[:, s, :]).then_inc(tile_stored[s], DMA)

            act.dma_start(weights[:, :, :], wc.rearrange("g c k -> c g k")).then_inc(weights_loaded, DMA)
            with act.Fori(0, LAST) as rnd:
                for s in range(SLOTS):
                    activate(rnd, s)
            for s in range(SLOTS):
                activate(LAST, s)


def kernel(x, L0_conv_wc):
    import numpy as np
    import concourse.bacc as bacc
    from concourse.bass_utils import run_bass_kernel_spmd

    nc = bacc.Bacc("TRN2", target_bir_lowering=False, num_devices=1)
    x = np.ascontiguousarray(x)
    wc = np.ascontiguousarray(L0_conv_wc)
    x_dram = nc.dram_tensor("x_dram", x.shape, mybir.dt.from_np(x.dtype), kind="ExternalInput").ap()
    wc_dram = nc.dram_tensor("wc_dram", wc.shape, mybir.dt.from_np(wc.dtype), kind="ExternalInput").ap()
    out_dram = nc.dram_tensor("out_dram", x.shape, mybir.dt.from_np(x.dtype), kind="ExternalOutput").ap()
    channel_mix_gelu(nc, x_dram, wc_dram, out_dram)
    r = run_bass_kernel_spmd(nc, [{"x_dram": x, "wc_dram": wc}], core_ids=[0])
    return r.results[0]["out_dram"]
```
